# Optimizing a Trainium2 kernel written in Bass

```python
import numpy as np
import jax
import jax.numpy as jnp

def _softmax(x, axis=-1):
    return jax.nn.softmax(x, axis=axis)

def _gelu(x):
    return jax.nn.gelu(x, approximate=True)

def _silu(x):
    return jax.nn.silu(x)

def _sigmoid(x):
    return jax.nn.sigmoid(x)

def _layernorm(x, axis=-1, eps=1e-05):
    m = jnp.mean(x, axis=axis, keepdims=True)
    v = jnp.var(x, axis=axis, keepdims=True)
    return (x - m) / jnp.sqrt(v + eps)

def _scatter_add(tgt, idx, src, axis=0):
    return tgt.at[idx].add(src)

def _segment_sum(src, seg, n):
    return jax.ops.segment_sum(src, seg, n)
kernel_name = 'mk_gnn_preln_d4_gnn_r16_c21db3'

def setup_inputs(seed: int=0):
    np.random.seed(seed)
    _w = jnp.asarray

    def _rec_inputs():
        import jax
        import jax.numpy as jnp
        _gk = jax.random.key(seed)
        x = -0.0003713 + 1 * jax.random.normal(jax.random.fold_in(_gk, 1), (3125, 128), jnp.float32)
        _s = jax.random.randint(jax.random.fold_in(_gk, 2), (50000,), 0, 3125, jnp.int32)
        _d = jax.random.randint(jax.random.fold_in(_gk, 3), (50000,), 0, 3125, jnp.int32)
        _loop = jnp.arange(3125, dtype=jnp.int32)
        src = jnp.concatenate([_s, _d, _loop])
        dst = jnp.concatenate([_d, _s, _loop])
        _o = jnp.argsort(dst, stable=True)
        src = src[_o]
        dst = dst[_o]
        edge_attr_128 = 9.41057e-06 + 1 * jax.random.normal(jax.random.fold_in(_gk, 12), (103125, 128), jnp.float32)
        return (x, src, dst, edge_attr_128)
    x, src, dst, edge_attr_128 = _rec_inputs()

    def _L0_gnn_setup():
        import jax, jax.numpy as jnp
        import numpy as np
        NEG_SLOPE = 0.2
        EPS = 1e-16
        N_NODES = 6250
        N_EDGES = 100000
        CHANNELS = 128
        M_LAYERS = 3

        def _gat_conv(x, src, dst, W, a_src, a_dst, b, n_nodes):
            h = x @ W
            s = h @ a_src
            d = h @ a_dst
            e = s[src] + d[dst]
            e = jnp.where(e > 0, e, NEG_SLOPE * e)
            e_max = jax.ops.segment_max(e, dst, num_segments=n_nodes)
            e_max = jnp.where(jnp.isfinite(e_max), e_max, 0.0)
            w = jnp.exp(e - e_max[dst])
            denom = jax.ops.segment_sum(w, dst, num_segments=n_nodes)
            alpha = w / (denom[dst] + EPS)
            out = jax.ops.segment_sum(alpha[:, None] * h[src], dst, num_segments=n_nodes)
            return out + b
        key = jax.random.key(seed)
        k1, k2, k3, k4, k5 = jax.random.split(key, 5)
        x = jax.random.normal(k1, (N_NODES, CHANNELS), dtype=jnp.float32)
        edge_index = jax.random.randint(k2, (2, N_EDGES), 0, N_NODES, dtype=jnp.int64)
        Ws = jax.random.normal(k3, (M_LAYERS, CHANNELS, CHANNELS), dtype=jnp.float32) / np.sqrt(CHANNELS)
        att_src = jax.random.normal(k4, (M_LAYERS, CHANNELS), dtype=jnp.float32) / np.sqrt(CHANNELS)
        att_dst = jax.random.normal(k5, (M_LAYERS, CHANNELS), dtype=jnp.float32) / np.sqrt(CHANNELS)
        bias = jnp.zeros((M_LAYERS, CHANNELS), dtype=jnp.float32)
        return {'x': x, 'edge_index': edge_index, 'Ws': Ws, 'att_src': att_src, 'att_dst': att_dst, 'bias': bias}
    _L0_gnn_all = _L0_gnn_setup()
    _L0_gnn_in = {k: v for k, v in _L0_gnn_all.items() if k in ('Ws', 'att_src', 'att_dst', 'bias')}
    del _L0_gnn_all

    def _L1_gnn_setup():
        import jax, jax.numpy as jnp
        import numpy as np
        N_NODES = 2500
        N_EDGES = 40000
        IN_FEATS = 128
        H_FEATS = 128

        def _sage_conv(h, src, dst, W_self, W_neigh, b, num_nodes):
            msg = h[src]
            agg = jax.ops.segment_sum(msg, dst, num_segments=num_nodes)
            deg = jax.ops.segment_sum(jnp.ones((src.shape[0],), h.dtype), dst, num_segments=num_nodes)
            h_neigh = agg / jnp.maximum(deg, 1.0)[:, None]
            return h @ W_self + h_neigh @ W_neigh + b
        key = jax.random.key(seed)
        ks = jax.random.split(key, 9)
        s = 1.0 / np.sqrt(IN_FEATS)
        return {'in_feat': jax.random.normal(ks[0], (N_NODES, IN_FEATS), jnp.float32), 'src': jax.random.randint(ks[1], (N_EDGES,), 0, N_NODES), 'dst': jax.random.randint(ks[2], (N_EDGES,), 0, N_NODES), 'W_self1': jax.random.normal(ks[3], (IN_FEATS, H_FEATS), jnp.float32) * s, 'W_neigh1': jax.random.normal(ks[4], (IN_FEATS, H_FEATS), jnp.float32) * s, 'b1': jnp.zeros((H_FEATS,), jnp.float32), 'W_self2': jax.random.normal(ks[5], (H_FEATS, H_FEATS), jnp.float32) * s, 'W_neigh2': jax.random.normal(ks[6], (H_FEATS, H_FEATS), jnp.float32) * s, 'b2': jnp.zeros((H_FEATS,), jnp.float32)}
    _L1_gnn_all = _L1_gnn_setup()
    _L1_gnn_in = {k: v for k, v in _L1_gnn_all.items() if k in ('W_self1', 'W_neigh1', 'b1', 'W_self2', 'W_neigh2', 'b2')}
    del _L1_gnn_all

    def _L2_gnn_setup():
        import jax, jax.numpy as jnp
        import numpy as np
        N = 6250
        E = 100000
        D = 128
        BN_EPS = 1e-05

        def _bn(v, g, b, m, var):
            return (v - m) * jax.lax.rsqrt(var + BN_EPS) * g + b
        key = jax.random.key(seed)
        ks = jax.random.split(key, 12)
        s = 1.0 / np.sqrt(D)
        return {'x': jax.random.normal(ks[0], (N, D), jnp.float32), 'edge_index': jax.random.randint(ks[1], (2, E), 0, N, jnp.int32), 'edge_attr': jax.random.normal(ks[2], (E, D), jnp.float32), 'gin_bn_g': jnp.ones((D,), jnp.float32), 'gin_bn_b': jnp.zeros((D,), jnp.float32), 'gin_bn_m': jax.random.normal(ks[3], (D,), jnp.float32) * 0.1, 'gin_bn_v': jax.random.uniform(ks[4], (D,), jnp.float32, 0.5, 1.5), 'gin_W': jax.random.normal(ks[5], (D, D), jnp.float32) * s, 'gin_b': jnp.zeros((D,), jnp.float32), 'bn1_g': jnp.ones((D,), jnp.float32), 'bn1_b': jnp.zeros((D,), jnp.float32), 'bn1_m': jax.random.normal(ks[6], (D,), jnp.float32) * 0.1, 'bn1_v': jax.random.uniform(ks[7], (D,), jnp.float32, 0.5, 1.5), 'ffn_W1': jax.random.normal(ks[8], (D, 2 * D), jnp.float32) * s, 'ffn_b1': jnp.zeros((2 * D,), jnp.float32), 'ffn_W2': jax.random.normal(ks[9], (2 * D, D), jnp.float32) / np.sqrt(2 * D), 'ffn_b2': jnp.zeros((D,), jnp.float32), 'bn2_g': jnp.ones((D,), jnp.float32), 'bn2_b': jnp.zeros((D,), jnp.float32), 'bn2_m': jax.random.normal(ks[10], (D,), jnp.float32) * 0.1, 'bn2_v': jax.random.uniform(ks[11], (D,), jnp.float32, 0.5, 1.5)}
    _L2_gnn_all = _L2_gnn_setup()
    _L2_gnn_in = {k: v for k, v in _L2_gnn_all.items() if k in ('gin_bn_g', 'gin_bn_b', 'gin_bn_m', 'gin_bn_v', 'gin_W', 'gin_b', 'bn1_g', 'bn1_b', 'bn1_m', 'bn1_v', 'ffn_W1', 'ffn_b1', 'ffn_W2', 'ffn_b2', 'bn2_g', 'bn2_b', 'bn2_m', 'bn2_v')}
    del _L2_gnn_all

    def _L3_gnn_setup():
        import jax, jax.numpy as jnp
        import numpy as np
        EPS = 0.0

        def _gin_conv(x, edge_index, W1, b1, W2, b2, n_nodes):
            src, dst = (edge_index[0], edge_index[1])
            agg = jax.ops.segment_sum(x[src], dst, num_segments=n_nodes)
            h = (1.0 + EPS) * x + agg
            h = jax.nn.relu(h @ W1 + b1)
            return h @ W2 + b2
        key = jax.random.key(seed)
        ks = jax.random.split(key, 10)
        N, E = (3125, 37500)
        d_in, d_hid, d_out = (128, 256, 128)
        x = jax.random.normal(ks[0], (N, d_in), dtype=jnp.float32)
        edge_index = jax.random.randint(ks[1], (2, E), 0, N, dtype=jnp.int64)

        def lin(k, fan_in, fan_out):
            bound = 1.0 / np.sqrt(fan_in)
            kw, kb = jax.random.split(k)
            W = jax.random.uniform(kw, (fan_in, fan_out), jnp.float32, -bound, bound)
            b = jax.random.uniform(kb, (fan_out,), jnp.float32, -bound, bound)
            return (W, b)
        W1a, b1a = lin(ks[2], d_in, d_hid)
        W2a, b2a = lin(ks[3], d_hid, d_hid)
        W1b, b1b = lin(ks[4], d_hid, d_hid)
        W2b, b2b = lin(ks[5], d_hid, d_out)
        return {'x': x, 'W1a': W1a, 'b1a': b1a, 'W2a': W2a, 'b2a': b2a, 'W1b': W1b, 'b1b': b1b, 'W2b': W2b, 'b2b': b2b, 'edge_index': edge_index}
    _L3_gnn_all = _L3_gnn_setup()
    _L3_gnn_in = {k: v for k, v in _L3_gnn_all.items() if k in ('W1a', 'b1a', 'W2a', 'b2a', 'W1b', 'b1b', 'W2b', 'b2b')}
    del _L3_gnn_all
    return {'x': x, 'src': src, 'dst': dst, 'edge_attr_128': edge_attr_128, 'L0_gnn_Ws': _L0_gnn_in['Ws'], 'L0_gnn_att_src': _L0_gnn_in['att_src'], 'L0_gnn_att_dst': _L0_gnn_in['att_dst'], 'L0_gnn_bias': _L0_gnn_in['bias'], 'L1_gnn_W_self1': _L1_gnn_in['W_self1'], 'L1_gnn_W_neigh1': _L1_gnn_in['W_neigh1'], 'L1_gnn_b1': _L1_gnn_in['b1'], 'L1_gnn_W_self2': _L1_gnn_in['W_self2'], 'L1_gnn_W_neigh2': _L1_gnn_in['W_neigh2'], 'L1_gnn_b2': _L1_gnn_in['b2'], 'L2_gnn_gin_bn_g': _L2_gnn_in['gin_bn_g'], 'L2_gnn_gin_bn_b': _L2_gnn_in['gin_bn_b'], 'L2_gnn_gin_bn_m': _L2_gnn_in['gin_bn_m'], 'L2_gnn_gin_bn_v': _L2_gnn_in['gin_bn_v'], 'L2_gnn_gin_W': _L2_gnn_in['gin_W'], 'L2_gnn_gin_b': _L2_gnn_in['gin_b'], 'L2_gnn_bn1_g': _L2_gnn_in['bn1_g'], 'L2_gnn_bn1_b': _L2_gnn_in['bn1_b'], 'L2_gnn_bn1_m': _L2_gnn_in['bn1_m'], 'L2_gnn_bn1_v': _L2_gnn_in['bn1_v'], 'L2_gnn_ffn_W1': _L2_gnn_in['ffn_W1'], 'L2_gnn_ffn_b1': _L2_gnn_in['ffn_b1'], 'L2_gnn_ffn_W2': _L2_gnn_in['ffn_W2'], 'L2_gnn_ffn_b2': _L2_gnn_in['ffn_b2'], 'L2_gnn_bn2_g': _L2_gnn_in['bn2_g'], 'L2_gnn_bn2_b': _L2_gnn_in['bn2_b'], 'L2_gnn_bn2_m': _L2_gnn_in['bn2_m'], 'L2_gnn_bn2_v': _L2_gnn_in['bn2_v'], 'L3_gnn_W1a': _L3_gnn_in['W1a'], 'L3_gnn_b1a': _L3_gnn_in['b1a'], 'L3_gnn_W2a': _L3_gnn_in['W2a'], 'L3_gnn_b2a': _L3_gnn_in['b2a'], 'L3_gnn_W1b': _L3_gnn_in['W1b'], 'L3_gnn_b1b': _L3_gnn_in['b1b'], 'L3_gnn_W2b': _L3_gnn_in['W2b'], 'L3_gnn_b2b': _L3_gnn_in['b2b']}

def reference(x, src, dst, edge_attr_128, L0_gnn_Ws, L0_gnn_att_src, L0_gnn_att_dst, L0_gnn_bias, L1_gnn_W_self1, L1_gnn_W_neigh1, L1_gnn_b1, L1_gnn_W_self2, L1_gnn_W_neigh2, L1_gnn_b2, L2_gnn_gin_bn_g, L2_gnn_gin_bn_b, L2_gnn_gin_bn_m, L2_gnn_gin_bn_v, L2_gnn_gin_W, L2_gnn_gin_b, L2_gnn_bn1_g, L2_gnn_bn1_b, L2_gnn_bn1_m, L2_gnn_bn1_v, L2_gnn_ffn_W1, L2_gnn_ffn_b1, L2_gnn_ffn_W2, L2_gnn_ffn_b2, L2_gnn_bn2_g, L2_gnn_bn2_b, L2_gnn_bn2_m, L2_gnn_bn2_v, L3_gnn_W1a, L3_gnn_b1a, L3_gnn_W2a, L3_gnn_b2a, L3_gnn_W1b, L3_gnn_b1b, L3_gnn_W2b, L3_gnn_b2b):
    import jax
    import jax.numpy as jnp

    def _L0_gnn_ref(x, edge_index, Ws, att_src, att_dst, bias):
        import jax, jax.numpy as jnp
        import numpy as np
        NEG_SLOPE = 0.2
        EPS = 1e-16
        N_NODES = 6250
        N_EDGES = 100000
        CHANNELS = 128
        M_LAYERS = 3

        def _gat_conv(x, src, dst, W, a_src, a_dst, b, n_nodes):
            h = x @ W
            s = h @ a_src
            d = h @ a_dst
            e = s[src] + d[dst]
            e = jnp.where(e > 0, e, NEG_SLOPE * e)
            e_max = jax.ops.segment_max(e, dst, num_segments=n_nodes)
            e_max = jnp.where(jnp.isfinite(e_max), e_max, 0.0)
            w = jnp.exp(e - e_max[dst])
            denom = jax.ops.segment_sum(w, dst, num_segments=n_nodes)
            alpha = w / (denom[dst] + EPS)
            out = jax.ops.segment_sum(alpha[:, None] * h[src], dst, num_segments=n_nodes)
            return out + b
        n = x.shape[0]
        loop = jnp.arange(n, dtype=edge_index.dtype)
        src = jnp.concatenate([edge_index[0], loop])
        dst = jnp.concatenate([edge_index[1], loop])
        for m in range(Ws.shape[0]):
            x = x + jax.nn.sigmoid(_gat_conv(x, src, dst, Ws[m], att_src[m], att_dst[m], bias[m], n))
        return x

    def _L1_gnn_ref(in_feat, src, dst, W_self1, W_neigh1, b1, W_self2, W_neigh2, b2):
        import jax, jax.numpy as jnp
        import numpy as np
        N_NODES = 2500
        N_EDGES = 40000
        IN_FEATS = 128
        H_FEATS = 128

        def _sage_conv(h, src, dst, W_self, W_neigh, b, num_nodes):
            msg = h[src]
            agg = jax.ops.segment_sum(msg, dst, num_segments=num_nodes)
            deg = jax.ops.segment_sum(jnp.ones((src.shape[0],), h.dtype), dst, num_segments=num_nodes)
            h_neigh = agg / jnp.maximum(deg, 1.0)[:, None]
            return h @ W_self + h_neigh @ W_neigh + b
        n = in_feat.shape[0]
        h = _sage_conv(in_feat, src, dst, W_self1, W_neigh1, b1, n)
        h = jax.nn.relu(h)
        h = _sage_conv(h, src, dst, W_self2, W_neigh2, b2, n)
        return h

    def _L2_gnn_ref(x, edge_index, edge_attr, gin_bn_g, gin_bn_b, gin_bn_m, gin_bn_v, gin_W, gin_b, bn1_g, bn1_b, bn1_m, bn1_v, ffn_W1, ffn_b1, ffn_W2, ffn_b2, bn2_g, bn2_b, bn2_m, bn2_v):
        import jax, jax.numpy as jnp
        import numpy as np
        N = 6250
        E = 100000
        D = 128
        BN_EPS = 1e-05

        def _bn(v, g, b, m, var):
            return (v - m) * jax.lax.rsqrt(var + BN_EPS) * g + b
        src, dst = (edge_index[0], edge_index[1])
        msg = jax.nn.relu(x[src] + edge_attr)
        aggr = jax.ops.segment_sum(msg, dst, num_segments=x.shape[0])
        h = x + aggr
        h = jax.nn.relu(_bn(h, gin_bn_g, gin_bn_b, gin_bn_m, gin_bn_v)) @ gin_W + gin_b
        h1 = _bn(x + h, bn1_g, bn1_b, bn1_m, bn1_v)
        ff = jax.nn.relu(h1 @ ffn_W1 + ffn_b1) @ ffn_W2 + ffn_b2
        return _bn(h1 + ff, bn2_g, bn2_b, bn2_m, bn2_v)

    def _L3_gnn_ref(x, W1a, b1a, W2a, b2a, W1b, b1b, W2b, b2b, edge_index):
        import jax, jax.numpy as jnp
        import numpy as np
        EPS = 0.0

        def _gin_conv(x, edge_index, W1, b1, W2, b2, n_nodes):
            src, dst = (edge_index[0], edge_index[1])
            agg = jax.ops.segment_sum(x[src], dst, num_segments=n_nodes)
            h = (1.0 + EPS) * x + agg
            h = jax.nn.relu(h @ W1 + b1)
            return h @ W2 + b2
        n_nodes = x.shape[0]
        h = _gin_conv(x, edge_index, W1a, b1a, W2a, b2a, n_nodes)
        h = jax.nn.relu(h)
        return _gin_conv(h, edge_index, W1b, b1b, W2b, b2b, n_nodes)
    edge_index = jnp.stack([src, dst])
    h = jnp.maximum(_layernorm(x, axis=-1), 0.0)
    x = x + _L0_gnn_ref(h, edge_index, L0_gnn_Ws, L0_gnn_att_src, L0_gnn_att_dst, L0_gnn_bias)
    h = jnp.maximum(_layernorm(x, axis=-1), 0.0)
    x = x + _L1_gnn_ref(h, src, dst, L1_gnn_W_self1, L1_gnn_W_neigh1, L1_gnn_b1, L1_gnn_W_self2, L1_gnn_W_neigh2, L1_gnn_b2)
    h = jnp.maximum(_layernorm(x, axis=-1), 0.0)
    x = x + _L2_gnn_ref(h, edge_index, edge_attr_128, L2_gnn_gin_bn_g, L2_gnn_gin_bn_b, L2_gnn_gin_bn_m, L2_gnn_gin_bn_v, L2_gnn_gin_W, L2_gnn_gin_b, L2_gnn_bn1_g, L2_gnn_bn1_b, L2_gnn_bn1_m, L2_gnn_bn1_v, L2_gnn_ffn_W1, L2_gnn_ffn_b1, L2_gnn_ffn_W2, L2_gnn_ffn_b2, L2_gnn_bn2_g, L2_gnn_bn2_b, L2_gnn_bn2_m, L2_gnn_bn2_v)
    h = jnp.maximum(_layernorm(x, axis=-1), 0.0)
    x = x + _L3_gnn_ref(h, L3_gnn_W1a, L3_gnn_b1a, L3_gnn_W2a, L3_gnn_b2a, L3_gnn_W1b, L3_gnn_b1b, L3_gnn_W2b, L3_gnn_b2b, edge_index)
    return x

_drawn_inputs = setup_inputs


def setup_inputs(seed=0):
    import zlib

    import numpy as np

    out = dict(_drawn_inputs(seed))
    spreads = {'L0_gnn_bias': (0.0, 0.8),
     'L1_gnn_b1': (0.0, 0.456),
     'L1_gnn_b2': (0.0, 0.321),
     'L2_gnn_gin_bn_g': (1.0, 0.2),
     'L2_gnn_gin_bn_b': (0.0, 2.0),
     'L2_gnn_gin_b': (0.0, 2.0),
     'L2_gnn_bn1_g': (1.0, 0.2),
     'L2_gnn_bn1_b': (0.0, 2.0),
     'L2_gnn_ffn_b1': (0.0, 2.0),
     'L2_gnn_ffn_b2': (0.0, 2.0),
     'L2_gnn_bn2_g': (1.0, 0.2),
     'L2_gnn_bn2_b': (0.0, 2.0)}
    factors = {'L0_gnn_att_src': 92.973,
     'L0_gnn_att_dst': 200.0,
     'L2_gnn_gin_bn_m': 8.0,
     'L2_gnn_bn1_m': 8.0,
     'L2_gnn_bn2_m': 23.152,
     'L3_gnn_b1a': 30.895,
     'L3_gnn_b2a': 8.0,
     'L3_gnn_b1b': 200.0,
     'L3_gnn_b2b': 64.0}
    for name, (base, spread) in spreads.items():
        noise = np.random.default_rng([zlib.crc32(name.encode()), seed]).standard_normal(out[name].shape)
        drawn = base * np.exp(spread * noise) if base else spread * noise
        out[name] = jnp.asarray(drawn.astype(out[name].dtype))
    for name, factor in factors.items():
        out[name] = (out[name] * factor).astype(out[name].dtype)
    return out
```

```python
from contextlib import ExitStack

import numpy as np

import concourse.bass as bass
from concourse import mybir

ALU = mybir.AluOpType
ACT = mybir.ActivationFunctionType
AX = mybir.AxisListType
F32 = mybir.dt.float32
F16 = mybir.dt.float16
BF16 = mybir.dt.bfloat16
F8 = mybir.dt.float8e4
I32 = mybir.dt.int32
U8 = mybir.dt.uint8
RMAX = bass.bass_isa.ReduceOp.max

P = 128
N = 3125
E = 103125
NB = -(-N // P)
TW, NT = 448, 7
ND = TW * NT
NP = NB * P
UE = 256
NU = 408
NG = NU // 2
EP = NU * UE
NC = EP // P
PAD_DST = 4000
WD = 32
NW = ND // WD
KW = WD * NB
UP, UJ = NU // 4, 4
LN_EPS = 1e-05
BN_EPS = 1e-05
GAT_EPS = 1e-16
SLOPE = 0.2
TOP = 55.0
GROUPS = [(g, 4 * g, min(4, NB - 4 * g)) for g in range(NT)]
SPANS = [(0, 9), (9, 17), (17, 25)]
SPAN_W = 9 * P

WEIGHTS = [("gatW", 3 * P), ("sWs1", P), ("sWn1", P), ("sWs2", P), ("sWn2", P), ("ginW", P), ("f1", 2 * P),
           ("f2a", P), ("f2b", P), ("w1a", 2 * P), ("w2a0", 2 * P), ("w2a1", 2 * P), ("w1b0", 2 * P),
           ("w1b1", 2 * P), ("w2b0", P), ("w2b1", P)]
COLUMNS = ["adst0", "adst1", "adst2", "sb1", "sb2", "g_g", "g_b", "g_m", "g_v", "ginb", "b1_g", "b1_b", "b1_m",
           "b1_v", "fb1a", "fb1b", "fb2", "b2_g", "b2_b", "b2_m", "b2_v", "b1a0", "b1a1", "b2a0", "b2a1",
           "b1b0", "b1b1", "b2b"]
ROWS = ["asrc0", "asrc1", "asrc2", "adst0", "adst1", "adst2", "gb0", "gb1", "gb2"]


def gnn_stack(nc, x_in, dst_units, dst_cols, src_cols, src_groups, edge_attr, weights, columns, rows, out):
    ctx = ExitStack()
    stage_sems = []
    with ctx:
        def sb(name, shape, dt):
            return ctx.enter_context(nc.sbuf_tensor(name, shape, dt))

        def sem(name):
            stage_sems.append(nc.alloc_semaphore(name=name))
            return stage_sems[-1]

        adj = sb("adj", [P, NB, ND], F8)
        x = sb("x", [P, NB, P], F32)
        y = sb("y", [P, NB, P], F32)
        yT = sb("yT", [P, NP], F32)
        zT = sb("zT", [P, NP], F32)
        parts = sb("parts", [P, 3, NB, P], BF16)
        arena = sb("arena", [P, 9216], F32)
        wts = sb("wts", [P, sum(w for _, w in WEIGHTS)], F32)
        cols = sb("cols", [P, len(COLUMNS)], F32)
        ident = sb("ident", [P, P], F32)
        ones = sb("ones", [P, P], F32)
        ones16 = sb("ones16", [P, P], BF16)
        iota_f = sb("iota_f", [P, P], F32)
        iota_h = sb("iota_h", [P, P], F16)
        pcol = sb("pcol", [P, 1], F32)
        dcol = sb("dcol", [P, NC], F32)
        window_tab = sb("window_tab", [1, 4 * NW], I32)
        block_tab = sb("block_tab", [1, 4 * NG], I32)
        neg128 = sb("neg128", [P, NB], F32)
        small = sb("small", [P, 512], F32)
        ps = ctx.enter_context(nc.psum_tensor("ps", [P, 8, 512], F32))

        W, at = {}, 0
        for name, width in WEIGHTS:
            W[name] = wts[:, at:at + width]
            at += width
        C = {name: cols[:, i:i + 1] for i, name in enumerate(COLUMNS)}
        zN = zT[:, :].rearrange("p (b c) -> p b c", c=P)
        hx = parts[:, :, :, :].rearrange("p a b c -> p (a b c)")[:, 0:2 * NB * 130].bitcast(F32)\
            .rearrange("p (b c) -> p b c", c=130)
        bounds_dram = nc.dram_tensor("bounds_dram", (2, NU), F32, kind="Internal").ap()
        ranges_dram = nc.dram_tensor("ranges_dram", (NW, 2), F32, kind="Internal").ap()
        h_dram = nc.dram_tensor("h_dram", (NP, P), F32, kind="Internal").ap()

        def load_and_tables():
            units = arena[0:UP, 0:UJ * UE].bitcast(I32)
            bounds = small[0:UP, 0:2 * UJ]
            brow = arena[0:NW, 1024:1024 + 2 * NU].rearrange("p (a u) -> p a u", a=2)
            mask = arena[0:NW, 2048:2048 + NU]
            pick = arena[0:NW, 2560:2560 + NU]
            up = arena[0:NW, 3072:3072 + NU]
            down = arena[0:NW, 3584:3584 + NU]
            t_b = small[0:NW, 16:18]
            rng = small[0:NW, 18:20]
            wrow = arena[0:1, 4096:4096 + 2 * NW]
            n_w, cum_w = small[0:1, 32:32 + NW], small[0:1, 160:160 + NW]
            wtab = arena[0:1, 4608:4608 + 4 * NW].rearrange("p (w k) -> p w k", k=4)
            gmin, gmax = arena[0:1, 5120:5120 + NG], arena[0:1, 5376:5376 + NG]
            gint = arena[0:1, 5632:5632 + 2 * NG].bitcast(I32)
            blo, bhi = arena[0:1, 6144:6144 + NG], arena[0:1, 6400:6400 + NG]
            n_g, cum_g = arena[0:1, 6656:6656 + NG], arena[0:1, 6912:6912 + NG]
            gtab = arena[0:1, 7168:7168 + 4 * NG].rearrange("p (w k) -> p w k", k=4)
            pint = small[:, 300:301].bitcast(I32)
            uint_row = small[:, 0:1]
            big_i = zT[:, 0:NU].bitcast(I32)

            s_units, s_x, s_w, s_made = sem("units_in"), sem("x_in"), sem("weights_in"), sem("consts_made")
            s_bounds, s_bout, s_bin = sem("bounds_made"), sem("bounds_out"), sem("bounds_back")
            s_rng, s_rout, s_rin, s_chain, s_fix = (sem("ranges_made"), sem("ranges_out"), sem("ranges_back"),
                                                    sem("table_chain"), sem("last_block_zero"))
            block = ctx_block("tables")

            @block.sync
            def _(sp):
                sp.dma_start(units, dst_units).then_inc(s_units, 16)
                sp.dma_start(dcol[:, :].bitcast(I32), dst_cols).then_inc(s_units, 16)
                sp.dma_start(x[:, :, :], x_in).then_inc(s_x, 16)
                sp.dma_start(wts[:, :], weights).then_inc(s_w, 16)
                sp.dma_start(cols[:, :], columns).then_inc(s_w, 16)
                sp.wait_ge(s_bounds, 2)
                sp.dma_start(bounds_dram.rearrange("a (p j) -> p a j", p=UP),
                             bounds.rearrange("p (a j) -> p a j", a=2)).then_inc(s_bout, 16)
                sp.wait_ge(s_bout, 16)
                sp.dma_start(brow, bounds_dram.unsqueeze(0).broadcast_to([NW, 2, NU]))\
                    .then_inc(s_bin, 16)
                sp.wait_ge(s_rng, 1)
                sp.dma_start(ranges_dram, rng).then_inc(s_rout, 16)
                sp.wait_ge(s_rout, 16)
                sp.dma_start(wrow, ranges_dram.rearrange("(o a) u -> o (a u)", o=1)).then_inc(s_rin, 16)
                sp.wait_ge(s_x, 16)
                sp.wait_ge(s_w, 32)

            @block.gpsimd
            def _(po):
                nc.gpsimd.iota(pint, [[0, 1]], base=0, channel_multiplier=1).then_inc(s_made, 1)
                nc.gpsimd.iota(big_i, [[1, NU]], base=0, channel_multiplier=0).then_inc(s_made, 1)
                nc.gpsimd.memset(ones[:, :], 1.0).then_inc(s_made, 1)
                nc.gpsimd.memset(ones16[:, :], 1.0).then_inc(s_made, 1)
                nc.gpsimd.memset(yT[:, ND:NP], 0.0).then_inc(s_made, 1)
                nc.gpsimd.memset(zT[:, ND:NP], 0.0).then_inc(s_made, 1)

            @block.vector
            def _(dve):
                done = [0]

                def chain(ins):
                    done[0] += 1
                    ins.then_inc(s_chain, 1)
                    dve.wait_ge(s_chain, done[0])

                dve.wait_ge(s_units, 32)
                u3 = units.rearrange("p (j e) -> p j e", j=UJ)
                nc.vector.tensor_reduce(bounds[:, 0:UJ], u3, AX.X, ALU.min).then_inc(s_bounds, 1)
                nc.vector.tensor_reduce(bounds[:, UJ:2 * UJ], u3, AX.X, ALU.max).then_inc(s_bounds, 1)
                chain(nc.vector.tensor_copy(arena[:, 8192:8192 + NC], dcol[:, :].bitcast(I32)))
                chain(nc.vector.tensor_copy(dcol[:, :], arena[:, 8192:8192 + NC]))
                dve.wait_ge(s_made, 6)
                chain(nc.vector.tensor_copy(pcol[:, :], pint))
                chain(nc.vector.tensor_copy(iota_f[:, :], big_i[:, 0:P]))
                chain(nc.vector.tensor_copy(iota_h[:, :], big_i[:, 0:P]))
                chain(nc.vector.tensor_scalar(ident[:, :], iota_f[:, :], pcol[:, 0:1], None, ALU.is_equal))
                chain(nc.vector.tensor_scalar(neg128[:, :], iota_f[:, 0:NB], -128.0, None, ALU.mult))
                chain(nc.vector.tensor_scalar(up, big_i[0:NW, :], 1.0, None, ALU.add))
                chain(nc.vector.tensor_scalar(down, up, -1.0, float(NU + 1), ALU.mult, ALU.add))
                chain(nc.vector.tensor_scalar(t_b[:, 0:1], pcol[0:NW, :], float(WD), None, ALU.mult))
                chain(nc.vector.tensor_scalar(t_b[:, 1:2], t_b[:, 0:1], float(WD - 1), None, ALU.add))
                dve.wait_ge(s_bin, 16)
                chain(nc.vector.tensor_scalar(mask, brow[:, 1, :], t_b[:, 0:1], None, ALU.is_ge))
                chain(nc.vector.scalar_tensor_tensor(out=mask, in0=brow[:, 0, :], scalar=t_b[:, 1:2], in1=mask,
                                                     op0=ALU.is_le, op1=ALU.mult))
                chain(nc.vector.tensor_tensor(pick, mask, up, ALU.mult))
                chain(nc.vector.tensor_reduce(rng[:, 1:2], pick, AX.X, ALU.max))
                chain(nc.vector.tensor_tensor(pick, mask, down, ALU.mult))
                chain(nc.vector.tensor_reduce(t_b[:, 0:1], pick, AX.X, ALU.max))
                chain(nc.vector.tensor_scalar(t_b[:, 1:2], t_b[:, 0:1], -1.0, float(NU), ALU.mult, ALU.add))
                chain(nc.vector.tensor_scalar(rng[:, 0:1], t_b[:, 1:2], float(NU - 2), None, ALU.min))
                chain(nc.vector.tensor_scalar(t_b[:, 0:1], rng[:, 0:1], 2.0, None, ALU.add))
                nc.vector.tensor_tensor(rng[:, 1:2], rng[:, 1:2], t_b[:, 0:1], ALU.max).then_inc(s_rng, 1)
                pair = brow[0:1, :, :].rearrange("p a (g t) -> p a g t", t=2)
                chain(nc.vector.tensor_reduce(gmin, pair[:, 0], AX.X, ALU.min))
                chain(nc.vector.tensor_reduce(gmax, pair[:, 1], AX.X, ALU.max))
                chain(nc.vector.tensor_scalar(gmin, gmin, float(N - 1), None, ALU.min))
                chain(nc.vector.tensor_copy(gint[:, 0:NG], gmin))
                chain(nc.vector.tensor_copy(gint[:, NG:2 * NG], gmax))
                chain(nc.vector.tensor_scalar(gint, gint, 7, None, ALU.arith_shift_right))
                chain(nc.vector.tensor_copy(blo, gint[:, 0:NG]))
                chain(nc.vector.tensor_scalar(bhi, gint[:, NG:2 * NG], 1.0, float(NB), ALU.add, ALU.min))
                chain(nc.vector.tensor_tensor(n_g, bhi, blo, ALU.subtract))
                chain(nc.vector.tensor_tensor_scan(cum_g, ones_row(NG), n_g, 0.0, ALU.mult, ALU.add))
                chain(nc.vector.tensor_tensor(gtab[:, :, 0], cum_g, n_g, ALU.subtract))
                chain(nc.vector.tensor_copy(gtab[:, :, 1], cum_g))
                chain(nc.vector.tensor_tensor(gtab[:, :, 2], blo, gtab[:, :, 0], ALU.subtract))
                chain(nc.vector.tensor_copy(gtab[:, :, 3], n_g))
                chain(nc.vector.tensor_copy(block_tab[:, :], gtab.rearrange("p w k -> p (w k)")))
                dve.wait_ge(s_rin, 16)
                w2 = wrow.rearrange("p (w k) -> p w k", k=2)
                chain(nc.vector.tensor_tensor(n_w, w2[:, :, 1], w2[:, :, 0], ALU.subtract))
                chain(nc.vector.tensor_tensor_scan(cum_w, ones_row(NW), n_w, 0.0, ALU.mult, ALU.add))
                chain(nc.vector.tensor_tensor(wtab[:, :, 0], cum_w, n_w, ALU.subtract))
                chain(nc.vector.tensor_copy(wtab[:, :, 1], cum_w))
                chain(nc.vector.tensor_tensor(wtab[:, :, 2], w2[:, :, 0], wtab[:, :, 0], ALU.subtract))
                chain(nc.vector.tensor_copy(wtab[:, :, 3], n_w))
                chain(nc.vector.tensor_copy(window_tab[:, :], wtab.rearrange("p w k -> p (w k)")))

            block_end(block)

        def ones_row(n):
            return ones[0:1, 0:1].broadcast_to([1, n])

        def build_adjacency():
            codes = arena[:, 0:400].bitcast(F16)
            src_i = arena[:, 400:400 + NC].bitcast(I32)
            block_i = arena[:, 1216:1216 + NC].bitcast(I32)
            slo = arena[:, 2032:2032 + NC]
            code = arena[:, 2848:2848 + NC]
            window0 = arena[:, 3664:3664 + NW]
            tmp = arena[:, 3776:3776 + NC]
            source_hot = [arena[:, 4608 + 64 * k:4672 + 64 * k].bitcast(F16) for k in range(2)]
            code_hot = [arena[:, 4736 + 400 * k:5136 + 400 * k].bitcast(F16) for k in range(2)]
            stage = [arena[:, 5536 + 200 * k:5736 + 200 * k].bitcast(F8).rearrange("p (s d) -> p s d", d=WD)
                     for k in range(2)]
            iw = zT[:, 0:KW].bitcast(I32)

            s_src, s_iota, s_chain, s_seen = sem("src_in"), sem("code_iota"), sem("code_chain"), sem("sums_seen")
            hot_ready = [sem(f"hot_ready{k}") for k in range(2)]
            hot_used = [sem(f"hot_used{k}") for k in range(2)]
            window_summed = [sem(f"window_summed{k}") for k in range(2)]
            window_staged = [sem(f"window_staged{k}") for k in range(2)]
            stage_stored = [sem(f"stage_stored{k}") for k in range(2)]
            block = ctx_block("build")

            def table(eng, w):
                base = eng.value_load(window_tab[0:1, bass.ds(w * 4, 1)], min_val=0, max_val=NU * NW)
                end = eng.value_load(window_tab[0:1, bass.ds(w * 4 + 1, 1)], min_val=1, max_val=NU * NW)
                return base, end

            @block.sync
            def _(sp):
                sp.dma_start(src_i, src_cols).then_inc(s_src, 16)
                sp.wait_ge(s_src, 16)

            @block.gpsimd
            def _(po):
                nc.gpsimd.iota(iw, [[1, KW]], base=0, channel_multiplier=0).then_inc(s_iota, 1)
                for k in range(2):
                    po.sem_inc(stage_stored[k], 1)
                with po.Fori(0, NW // 2) as j:
                    for k in range(2):
                        po.wait_ge(window_staged[k], j + 2)
                        nc.gpsimd.tensor_copy(adj[:, :, bass.ds(j * 2 * WD + k * WD, WD)].bitcast(U8),
                                              stage[k].bitcast(U8)).then_inc(stage_stored[k], 1)

            @block.scalar
            def _(act):
                for k in range(2):
                    act.sem_inc(window_staged[k], 1)
                with act.Fori(0, NW // 2) as j:
                    for k in range(2):
                        act.wait_ge(window_summed[k], j + 1)
                        act.wait_ge(stage_stored[k], j + 1)
                        act.sem_inc(s_seen, 1)
                        for h in range(2):
                            last = nc.scalar.activation(
                                stage[k][:, :, 16 * h:16 * h + 16].rearrange("p s d -> p d s"),
                                ps[:, 2 * k + h, 0:16 * NB].rearrange("p (d s) -> p d s", s=NB),
                                ACT.Copy, saturate=False)
                        last.then_inc(window_staged[k], 1)

            @block.vector
            def _(dve):
                done = [0]

                def chain(ins):
                    done[0] += 1
                    ins.then_inc(s_chain, 1)
                    dve.wait_ge(s_chain, done[0])

                dve.wait_ge(s_iota, 1)
                dve.wait_ge(s_src, 16)
                chain(nc.vector.tensor_copy(codes, iw))
                chain(nc.vector.tensor_scalar(window0, iw[:, 0:NW], float(KW), None, ALU.mult))
                chain(nc.vector.tensor_scalar(block_i, src_i, 7, None, ALU.arith_shift_right))
                chain(nc.vector.tensor_copy(tmp, block_i))
                chain(nc.vector.scalar_tensor_tensor(out=slo, in0=tmp, scalar=-128.0, in1=src_i,
                                                     op0=ALU.mult, op1=ALU.add))
                chain(nc.vector.scalar_tensor_tensor(out=code, in0=dcol[:, :], scalar=float(NB), in1=tmp,
                                                     op0=ALU.mult, op1=ALU.add))
                with dve.Fori(0, NW) as w:
                    base, end = table(dve, w)
                    shift = dve.value_load(window_tab[0:1, bass.ds(w * 4 + 2, 1)], min_val=-NU * NW, max_val=NU)
                    with dve.Fori(base, end) as step:
                        for k in range(2):
                            c = nc.s_assert_within(step + shift, 0, NU - 1, skip_runtime_bounds_check_because="the table holds units only") * 2 + k
                            dve.wait_ge(hot_used[k], step + 1)
                            nc.vector.tensor_scalar(source_hot[k], iota_h[:, :], slo[:, bass.ds(c, 1)], None,
                                                    ALU.is_equal)
                            nc.vector.tensor_scalar(code_hot[k], codes, window0[:, bass.ds(w, 1)],
                                                    code[:, bass.ds(c, 1)], ALU.add,
                                                    ALU.is_equal).then_inc(hot_ready[k], 1)

            @block.tensor
            def _(pe):
                for k in range(2):
                    pe.sem_inc(hot_used[k], 1)
                with pe.Fori(0, NW // 2) as j:
                    for b in range(2):
                        base, end = table(pe, j * 2 + b)
                        pe.wait_ge(window_staged[b], j + 1)

                        def unit(step, first):
                            for k in range(2):
                                pe.wait_ge(hot_ready[k], step + 1)
                                for h in range(2):
                                    last = nc.tensor.matmul(ps[:, 2 * b + h, 0:16 * NB], source_hot[k],
                                                            code_hot[k][:, 16 * NB * h:16 * NB * (h + 1)],
                                                            start=first and k == 0, stop=False,
                                                            skip_group_check=True)
                                last.then_inc(hot_used[k], 1)

                        unit(base, True)
                        with pe.Fori(base + 1, end) as step:
                            unit(step, False)
                        pe.drain().then_inc(window_summed[b], 1)

            block_end(block)

        def self_loops(name, sign):
            s_d = sem(name)
            block = ctx_block(name)

            @block.vector
            def _(dve):
                for i in range(NB):
                    d1 = min(P * i + P, ND)
                    n = d1 - P * i
                    nc.vector.tensor_tensor(adj[:, i, P * i:d1], adj[:, i, P * i:d1], ident[:, 0:n],
                                            ALU.add if sign > 0 else ALU.subtract, saturate=False)\
                        .then_inc(s_d, 1)
                dve.wait_ge(s_d, NB)

            block_end(block)

        def layernorm(name):
            stats = arena[:, 0:6 * NB].rearrange("p (b k) -> p b k", k=6)
            mv = arena[:, 160:160 + 2 * NB].rearrange("p (b k) -> p b k", k=2)
            var = arena[:, 224:224 + NB]
            sd = arena[:, 256:256 + NB]
            rstd = arena[:, 288:288 + NB]
            s_chain, s_sd, s_norm, s_relu = (sem(name + "_chain"), sem(name + "_sd"), sem(name + "_norm"),
                                             sem(name + "_relu"))
            s_t, s_c = sem(name + "_turned"), sem(name + "_copied")
            block = ctx_block(name)

            @block.vector
            def _(dve):
                for i in range(NB):
                    nc.vector.bn_stats(stats[:, i, :], x[:, i, :]).then_inc(s_chain, 1)
                dve.wait_ge(s_chain, NB)
                for i in range(NB):
                    nc.vector.bn_aggr(mv[:, i, :], stats[:, i, :]).then_inc(s_chain, 1)
                dve.wait_ge(s_chain, 2 * NB)
                nc.vector.tensor_scalar(var, mv[:, :, 1], LN_EPS, None, ALU.add).then_inc(s_chain, 1)
                dve.wait_ge(s_sd, 1)
                nc.vector.reciprocal(rstd, sd).then_inc(s_chain, 1)
                dve.wait_ge(s_chain, 2 * NB + 2)
                for i in range(NB):
                    nc.vector.tensor_scalar(y[:, i, :], x[:, i, :], mv[:, i, 0:1], rstd[:, i:i + 1],
                                            ALU.subtract, ALU.mult).then_inc(s_norm, 1)
                for g, b0, n in GROUPS:
                    dve.wait_ge(s_t, g + 1)
                    nc.vector.tensor_copy(yT[:, P * b0:P * (b0 + n)], ps[:, g, 0:P * n]).then_inc(s_c, 1)
                dve.wait_ge(s_c, NT)

            @block.scalar
            def _(act):
                act.wait_ge(s_chain, 2 * NB + 1)
                nc.scalar.activation(sd, var, ACT.Sqrt).then_inc(s_sd, 1)
                for g, b0, n in GROUPS:
                    act.wait_ge(s_norm, b0 + n)
                    nc.scalar.activation(y[:, b0:b0 + n, :], y[:, b0:b0 + n, :], ACT.Relu).then_inc(s_relu, 1)

            @block.tensor
            def _(pe):
                turn_blocks(pe, y, s_relu, s_t)

            block_end(block)

        def turn_blocks(pe, source, ready, turned):
            for g, b0, n in GROUPS:
                if ready is not None:
                    pe.wait_ge(ready, g + 1)
                for i in range(n):
                    last = nc.tensor.transpose(ps[:, g, P * i:P * i + P], source[:, b0 + i, :], ident[:, :])
                last.then_inc(turned, 1)

        def node_major(name, source, target, add, store=None):
            s_t, s_c, s_o = sem(name + "_turned"), sem(name + "_copied"), sem(name + "_out")
            block = ctx_block(name)

            @block.tensor
            def _(pe):
                turn_blocks(pe, source.rearrange("p (b c) -> p b c", c=P), None, s_t)

            @block.vector
            def _(dve):
                for g, b0, n in GROUPS:
                    dve.wait_ge(s_t, g + 1)
                    src = ps[:, g, 0:P * n].rearrange("p (b c) -> p b c", c=P)
                    if add:
                        nc.vector.tensor_tensor(target[:, b0:b0 + n, :], src, target[:, b0:b0 + n, :],
                                                ALU.add).then_inc(s_c, 1)
                    else:
                        nc.vector.tensor_copy(target[:, b0:b0 + n, :], src).then_inc(s_c, 1)
                dve.wait_ge(s_c, NT)

            if store is not None:
                @block.sync
                def _(sp):
                    for g, b0, n in GROUPS:
                        sp.wait_ge(s_c, g + 1)
                        sp.dma_start(store[:, b0:b0 + n, :], target[:, b0:b0 + n, :]).then_inc(s_o, 16)
                    sp.wait_ge(s_o, 16 * NT)

            block_end(block)

        def neighbour_sums(name, source, target, finish=None):
            CH, NCH = 5, 5
            rest = [arena[:, 6656 + 640 * k:7296 + 640 * k].rearrange("p (b c) -> p b c", c=P) for k in range(2)]
            s_hi, s_r, s_mid, s_lo = (sem(name + "_hi"), sem(name + "_rest"), sem(name + "_mid"),
                                      sem(name + "_lo"))
            s_sum, s_z = sem(name + "_summed"), sem(name + "_z")
            block = ctx_block(name)

            @block.scalar
            def _(act):
                for c in range(NCH):
                    nc.scalar.copy(parts[:, 0, CH * c:CH * c + CH, :], source[:, CH * c:CH * c + CH, :])\
                        .then_inc(s_hi, 1)
                    act.wait_ge(s_r, c + 1)
                    nc.scalar.copy(parts[:, 1, CH * c:CH * c + CH, :], rest[c % 2]).then_inc(s_mid, 1)

            @block.vector
            def _(dve):
                for c in range(NCH):
                    b = slice(CH * c, CH * c + CH)
                    dve.wait_ge(s_hi, c + 1)
                    if c >= 2:
                        dve.wait_ge(s_lo, c - 1)
                    nc.vector.tensor_tensor(rest[c % 2], source[:, b, :], parts[:, 0, b, :], ALU.subtract)\
                        .then_inc(s_r, 1)
                    dve.wait_ge(s_mid, c + 1)
                    nc.vector.tensor_tensor(parts[:, 2, b, :], rest[c % 2], parts[:, 1, b, :], ALU.subtract)\
                        .then_inc(s_lo, 1)
                for t in range(NT):
                    dve.wait_ge(s_sum, t + 1)
                    tile = slice(TW * t, TW * t + TW)
                    if finish is None:
                        nc.vector.tensor_copy(target[:, tile], ps[:, t, 0:TW]).then_inc(s_z, 1)
                    else:
                        op, other = finish
                        nc.vector.tensor_tensor(target[:, tile], ps[:, t, 0:TW], other[:, tile], op)\
                            .then_inc(s_z, 1)
                dve.wait_ge(s_z, NT)

            @block.tensor
            def _(pe):
                for i in range(NB):
                    if i % CH == 0:
                        pe.wait_ge(s_lo, i // CH + 1)
                    for k in range(3):
                        for t in range(NT):
                            mm = nc.tensor.matmul(ps[:, t, 0:TW], parts[:, k, i, :], adj[:, i, TW * t:TW * t + TW],
                                                  start=(i == 0 and k == 0), stop=(i == NB - 1 and k == 2))
                            if i == NB - 1 and k == 2:
                                mm.then_inc(s_sum, 1)

            block_end(block)

        def gat_layer(l):
            d_row = arena[:, 0:ND]
            m_row = arena[:, ND:2 * ND]
            work = [zT[:, 0:SPAN_W], zT[:, SPAN_W:2 * SPAN_W], arena[:, 2 * ND:2 * ND + SPAN_W],
                    arena[:, 2 * ND + SPAN_W:2 * ND + 2 * SPAN_W]]
            asrc_row, adst_row, adst_all, junk = (arena[:, 6400 + P * k:6528 + P * k] for k in range(4))
            diag = [arena[:, 6400 + P * k:6528 + P * k] for k in range(2)]
            bias_row = arena[:, 8704:8832]
            s_col, s8, s2, sq, d_col, m_col, rd = (small[:, 32 * k:32 * k + NB] for k in range(7))
            ext = small[:, 256:264]
            n = f"gat{l}_"
            s_rows, s_cst, s_h, s_he, s_hT, s_hTe, s_d, s_de = (sem(n + k) for k in
                ("rows_in", "consts", "h_made", "h_copied", "hT_made", "hT_copied", "d_made", "d_copied"))
            block = ctx_block(n + "project")

            @block.sync
            def _(sp):
                for k, buf in enumerate((asrc_row, adst_row, bias_row)):
                    sp.dma_start(buf, rows[l + 3 * k:l + 3 * k + 1, :].broadcast_to([P, P])).then_inc(s_rows, 16)
                sp.wait_ge(s_rows, 48)

            @block.tensor
            def _(pe):
                w = W["gatW"][:, P * l:P * l + P]
                for g, b0, m in GROUPS:
                    for i in range(m):
                        mm = nc.tensor.matmul(ps[:, g, P * i:P * i + P], yT[:, P * (b0 + i):P * (b0 + i) + P], w,
                                              start=True, stop=True)
                    mm.then_inc(s_h, 1)
                for t in range(NT):
                    pe.wait_ge(s_he, t + 1)
                    nc.tensor.matmul(ps[:, t, 0:TW], w, yT[:, TW * t:TW * t + TW], start=True, stop=True)\
                        .then_inc(s_hT, 1)
                pe.wait_ge(s_cst, 1)
                for t in range(NT):
                    pe.wait_ge(s_hTe, t + 1)
                    nc.tensor.matmul(ps[:, t, 0:TW], adst_all, zT[:, TW * t:TW * t + TW], start=True, stop=True)\
                        .then_inc(s_d, 1)

            @block.scalar
            def _(act):
                for t in range(NT):
                    act.wait_ge(s_hT, t + 1)
                    nc.scalar.copy(zT[:, TW * t:TW * t + TW], ps[:, t, 0:TW]).then_inc(s_hTe, 1)
                for t in range(NT):
                    act.wait_ge(s_d, t + 1)
                    nc.scalar.copy(d_row[:, TW * t:TW * t + TW], ps[:, t, 0:TW]).then_inc(s_de, 1)
                act.wait_ge(s_de, NT)

            @block.vector
            def _(dve):
                nc.vector.memset(hx[:, :, P:P + 1], 1.0)
                nc.vector.memset(m_row, 0.0)
                nc.vector.tensor_copy(adst_all, C[f"adst{l}"].broadcast_to([P, P])).then_inc(s_cst, 1)
                for g, b0, m in GROUPS:
                    dve.wait_ge(s_h, g + 1)
                    nc.vector.tensor_copy(hx[:, b0:b0 + m, 0:P],
                                          ps[:, g, 0:P * m].rearrange("p (b c) -> p b c", c=P)).then_inc(s_he, 1)
                dve.wait_ge(s_rows, 48)
                dve.wait_ge(s_he, NT)
                for i in range(NB):
                    for k, (row, col) in enumerate(((asrc_row, s_col), (adst_row, d_col))):
                        if i + k:
                            dve.wait_ge(s_cst, 1 + 2 * i + k)
                        nc.vector.tensor_tensor_reduce(junk, hx[:, i, 0:P], row, 1.0, 0.0, ALU.mult, ALU.add,
                                                       col[:, i:i + 1]).then_inc(s_cst, 1)

            block_end(block)

            s_ch, s_pool, s_mx, s_t, s_red, s_mc, s_dg, s_b, s_v = (sem(n + k) for k in
                ("chain", "range_all", "max_step", "max_turned", "max_reduced", "m_col", "diag", "m_spread", "v_row"))
            block = ctx_block(n + "maximum")

            @block.gpsimd
            def _(po):
                po.wait_ge(s_ch, 3)
                nc.gpsimd.partition_all_reduce(ext[:, 2:4], ext[:, 0:2], P, RMAX).then_inc(s_pool, 1)

            @block.tensor
            def _(pe):
                pe.wait_ge(s_mx, 2 * NB)
                for g, b0, m in GROUPS:
                    for i in range(m):
                        c = P * (b0 + i)
                        k = min(P, ND - c)
                        mm = nc.tensor.transpose(ps[0:k, g, P * i:P * i + P], m_row[:, c:c + k], ident[:, :])
                    mm.then_inc(s_t, 1)
                for i in range(NB):
                    k = min(P, ND - P * i)
                    pe.wait_ge(s_dg, i + 1)
                    nc.tensor.matmul(ps[:, i // 4, P * (i % 4):P * (i % 4) + k], ones[:, :], diag[i % 2][:, 0:k],
                                     start=True, stop=True).then_inc(s_b, 1)

            @block.vector
            def _(dve):
                done = [0]

                def chain(ins):
                    done[0] += 1
                    ins.then_inc(s_ch, 1)
                    dve.wait_ge(s_ch, done[0])

                chain(nc.vector.tensor_reduce(ext[:, 0:1], s_col, AX.X, ALU.max))
                chain(nc.vector.tensor_reduce(ext[:, 4:5], s_col, AX.X, ALU.min))
                chain(nc.vector.tensor_scalar(ext[:, 1:2], ext[:, 4:5], -1.0, None, ALU.mult))
                dve.wait_ge(s_pool, 1)
                chain(nc.vector.tensor_tensor(ext[:, 5:6], ext[:, 2:3], ext[:, 3:4], ALU.add))
                chain(nc.vector.tensor_scalar(ext[:, 5:6], ext[:, 5:6], 1e-20, 1.0 / TOP, ALU.max, ALU.mult))
                chain(nc.vector.reciprocal(ext[:, 6:7], ext[:, 5:6]))
                chain(nc.vector.tensor_scalar(sq, s_col, ext[:, 3:4], ext[:, 6:7], ALU.add, ALU.mult))
                chain(nc.vector.tensor_scalar(sq, sq, 0.5, None, ALU.add))
                chain(nc.vector.tensor_scalar(s8, s_col, 1.0 - SLOPE, None, ALU.mult))
                chain(nc.vector.tensor_scalar(s2, s_col, SLOPE, None, ALU.mult))
                for i in range(NB):
                    for h in range(2):
                        c0, c1 = (ND // 2 * h, ND // 2 * (h + 1))
                        if i:
                            dve.wait_ge(s_mx, 2 * i - 1 + h)
                        nc.vector.scalar_tensor_tensor(out=m_row[:, c0:c1], in0=adj[:, i, c0:c1].bitcast(U8),
                                                       scalar=sq[:, i:i + 1], in1=m_row[:, c0:c1],
                                                       op0=ALU.min, op1=ALU.max).then_inc(s_mx, 1)
                nc.vector.memset(m_col, 0.0).then_inc(s_red, 1)
                dve.wait_ge(s_red, 1)
                for g, b0, m in GROUPS:
                    dve.wait_ge(s_t, g + 1)
                    k = P if g < NT - 1 else ND - P * b0
                    nc.vector.tensor_reduce(m_col[0:k, b0:b0 + m],
                                            ps[0:k, g, 0:P * m].rearrange("p (b c) -> p b c", c=P),
                                            AX.X, ALU.max).then_inc(s_red, 1)
                dve.wait_ge(s_red, 1 + NT)
                chain(nc.vector.tensor_scalar(m_col, m_col, -0.5, ext[:, 5:6], ALU.add, ALU.mult))
                chain(nc.vector.tensor_scalar(m_col, m_col, ext[:, 3:4], None, ALU.subtract))
                chain(nc.vector.tensor_tensor(m_col, m_col, d_col, ALU.add))
                chain(nc.vector.scalar_tensor_tensor(out=m_col, in0=m_col, scalar=SLOPE, in1=m_col,
                                                     op0=ALU.mult, op1=ALU.max))
                for i in range(NB):
                    if i >= 2:
                        dve.wait_ge(s_b, i - 1)
                    nc.vector.tensor_scalar(diag[i % 2], ident[:, :], m_col[:, i:i + 1], None, ALU.mult)\
                        .then_inc(s_dg, 1)
                dve.wait_ge(s_b, NB)
                for g, b0, m in GROUPS:
                    c0, c1 = P * b0, min(P * (b0 + m), ND)
                    nc.vector.scalar_tensor_tensor(out=m_row[:, c0:c1], in0=d_row[:, c0:c1], scalar=SLOPE,
                                                   in1=ps[:, g, 0:c1 - c0], op0=ALU.mult,
                                                   op1=ALU.subtract).then_inc(s_v, 1)
                dve.wait_ge(s_v, NT)

            block_end(block)

            s_R, s_T, s_c, s_E, s_w, s_mm, s_den, s_o, s_sg, s_y = (sem(n + k) for k in
                ("relu", "shifted", "clamped", "exp", "weight", "summed", "den", "conv", "sigmoid", "y_new"))
            block = ctx_block(n + "attend")
            conv = yT[:, :].rearrange("p (b c) -> p b c", c=P)
            steps = [(h, i) for h in range(len(SPANS)) for i in range(NB)]
            NQ, NBUF = len(steps), len(work)

            def span(h):
                return P * SPANS[h][0], min(P * SPANS[h][1], ND)

            def buf(q):
                c0, c1 = span(steps[q][0])
                return work[q % NBUF][:, 0:c1 - c0]

            def place(b):
                h = [k for k, (b0, b1) in enumerate(SPANS) if b0 <= b < b1][0]
                j = b - SPANS[h][0]
                return (3 * h + j // 3) % 8, 129 * (j % 3)

            def span_out(dve, b0, b1, summed):
                dve.wait_ge(s_mm, summed)
                size = [min(P, ND - P * b) for b in range(b0, b1)]
                for b, k in zip(range(b0, b1), size):
                    bank, c = place(b)
                    nc.vector.tensor_scalar(rd[0:k, b:b + 1], ps[0:k, bank, c + P:c + P + 1], GAT_EPS, None,
                                            ALU.add).then_inc(s_den, 1)
                dve.wait_ge(s_den, b0 + b1)
                for b, k in zip(range(b0, b1), size):
                    nc.vector.reciprocal(rd[0:k, b:b + 1], rd[0:k, b:b + 1]).then_inc(s_den, 1)
                dve.wait_ge(s_den, 2 * b1)
                for b, k in zip(range(b0, b1), size):
                    bank, c = place(b)
                    nc.vector.scalar_tensor_tensor(out=conv[0:k, b, :], in0=ps[0:k, bank, c:c + P],
                                                   scalar=rd[0:k, b:b + 1], in1=bias_row[0:k, :], op0=ALU.mult,
                                                   op1=ALU.add).then_inc(s_o, 1)

            @block.tensor
            def _(pe):
                for q, (h, i) in enumerate(steps):
                    b0, b1 = SPANS[h]
                    pe.wait_ge(s_w, q + 1)
                    if (h, i) == (2, 0):
                        pe.wait_ge(s_o, SPANS[0][1])
                    for b in range(b0, b1):
                        bank, c = place(b)
                        k = min(P, ND - P * b)
                        o = P * (b - b0)
                        mm = nc.tensor.matmul(ps[0:k, bank, c:c + 129], work[q % NBUF][:, o:o + k], hx[:, i, 0:129],
                                              start=(i == 0 and (b - b0) % 3 == 0), stop=(i == NB - 1),
                                              skip_group_check=True)
                    mm.then_inc(s_mm, 1)

            @block.scalar
            def _(act):
                for q in range(NQ + 2):
                    if q < NQ:
                        h, i = steps[q]
                        c0, c1 = span(h)
                        if q >= NBUF:
                            act.wait_ge(s_mm, q - NBUF + 1)
                        nc.scalar.activation(buf(q), d_row[:, c0:c1], ACT.Relu, bias=s8[:, i:i + 1],
                                             scale=1.0 - SLOPE).then_inc(s_R, 1)
                    if q >= 2:
                        act.wait_ge(s_c, q - 1)
                        nc.scalar.activation(buf(q - 2), buf(q - 2), ACT.Exp).then_inc(s_E, 1)
                act.wait_ge(s_o, NB)
                for g, b0, m in GROUPS:
                    nc.scalar.activation(conv[:, b0:b0 + m, :], conv[:, b0:b0 + m, :], ACT.Sigmoid).then_inc(s_sg, 1)

            @block.gpsimd
            def _(po):
                for q in range(NQ):
                    po.wait_ge(s_T, q + 1)
                    nc.gpsimd.tensor_scalar(buf(q), buf(q), 0.0, -200.0, ALU.min, ALU.max).then_inc(s_c, 1)

            @block.vector
            def _(dve):
                for q in range(NQ + 2):
                    if q < NQ:
                        h, i = steps[q]
                        c0, c1 = span(h)
                        dve.wait_ge(s_R, q + 1)
                        nc.vector.scalar_tensor_tensor(out=buf(q), in0=m_row[:, c0:c1], scalar=s2[:, i:i + 1],
                                                       in1=buf(q), op0=ALU.add, op1=ALU.add).then_inc(s_T, 1)
                    if q >= 2:
                        h, i = steps[q - 2]
                        c0, c1 = span(h)
                        dve.wait_ge(s_E, q - 1)
                        nc.vector.tensor_tensor(buf(q - 2), buf(q - 2), adj[:, i, c0:c1], ALU.mult).then_inc(s_w, 1)
                    if q >= 4 and (q - 4) % NB == NB - 1:
                        b0, b1 = SPANS[(q - 4) // NB]
                        span_out(dve, b0, b1, q - 3)
                span_out(dve, *SPANS[-1], NQ)
                for g, b0, m in GROUPS:
                    dve.wait_ge(s_sg, g + 1)
                    nc.vector.tensor_tensor(y[:, b0:b0 + m, :], y[:, b0:b0 + m, :], conv[:, b0:b0 + m, :],
                                            ALU.add).then_inc(s_y, 1)
                dve.wait_ge(s_y, NT)

            block_end(block)

        def add_y_to_x(name):
            s_d = sem(name)
            block = ctx_block(name)

            @block.vector
            def _(dve):
                nc.vector.tensor_tensor(x[:, :, :], x[:, :, :], y[:, :, :], ALU.add).then_inc(s_d, 1)
                dve.wait_ge(s_d, 1)

            block_end(block)

        def turn_y(name, source, target):
            s_t, s_c = sem(name + "_turned"), sem(name + "_copied")
            block = ctx_block(name)

            @block.tensor
            def _(pe):
                turn_blocks(pe, source, None, s_t)

            @block.vector
            def _(dve):
                for g, b0, m in GROUPS:
                    dve.wait_ge(s_t, g + 1)
                    nc.vector.tensor_copy(target[:, P * b0:P * (b0 + m)], ps[:, g, 0:P * m]).then_inc(s_c, 1)
                dve.wait_ge(s_c, NT)

            block_end(block)

        def degrees(name, rdeg):
            s_m, s_x, s_r = sem(name + "_summed"), sem(name + "_max"), sem(name + "_r")
            block = ctx_block(name)

            @block.tensor
            def _(pe):
                for i in range(NB):
                    for t in range(NT):
                        mm = nc.tensor.matmul(ps[:, t, 0:TW], ones16[:, :], adj[:, i, TW * t:TW * t + TW],
                                              start=(i == 0), stop=(i == NB - 1))
                        if i == NB - 1:
                            mm.then_inc(s_m, 1)

            @block.vector
            def _(dve):
                for t in range(NT):
                    tile = slice(TW * t, TW * t + TW)
                    dve.wait_ge(s_m, t + 1)
                    nc.vector.tensor_scalar(rdeg[:, tile], ps[:, t, 0:TW], 1.0, None, ALU.max).then_inc(s_x, 1)
                    dve.wait_ge(s_x, t + 1)
                    nc.vector.reciprocal(rdeg[:, tile], rdeg[:, tile]).then_inc(s_r, 1)
                dve.wait_ge(s_r, NT)

            block_end(block)

        def dense(name, layers, clear=()):
            flat = [(t, q, outs) for t in range(NT) for q, layer in enumerate(layers) for outs in layer]
            s_mm, s_wr = sem(name + "_made"), sem(name + "_stored")
            block = ctx_block(name)
            sizes = [len(layer) for layer in layers]

            if clear:
                s_clr = sem(name + "_cleared")

                @block.vector
                def _(dve):
                    for k, buf in enumerate(clear):
                        nc.vector.memset(buf[:, ND:NP], 0.0).then_inc(s_clr, 1)
                    dve.wait_ge(s_clr, len(clear))

            @block.tensor
            def _(pe):
                at = 0
                for q, layer in enumerate(layers):
                    for t in range(NT):
                        for o, (products, write) in enumerate(layer):
                            need = at - 7
                            if q:
                                before = sum(sizes[:q - 1]) * NT + sizes[q - 1] * (t + 1)
                                need = max(need, before)
                            if need > 0:
                                pe.wait_ge(s_wr, need)
                            for j, (w, inp) in enumerate(products):
                                mm = nc.tensor.matmul(ps[:, at % 8, 0:TW], w, inp[:, TW * t:TW * t + TW],
                                                      start=(j == 0), stop=(j == len(products) - 1))
                            mm.then_inc(s_mm, 1)
                            at += 1

            @block.scalar
            def _(act):
                at = 0
                for q, layer in enumerate(layers):
                    for t in range(NT):
                        for o, (products, write) in enumerate(layer):
                            act.wait_ge(s_mm, at + 1)
                            func, bias, scale, target = write
                            nc.scalar.activation(target[:, TW * t:TW * t + TW], ps[:, at % 8, 0:TW], func, bias=bias,
                                                 scale=scale).then_inc(s_wr, 1)
                            at += 1
                act.wait_ge(s_wr, at)

            block_end(block)

        def edge_messages():
            SL = 4
            attr = [arena[:, 512 * s:512 * s + 512] for s in range(SL)]
            got = [arena[:, 2048 + 512 * s:2560 + 512 * s] for s in range(SL)]
            idx = [arena[:, 4096 + 4 * s:4100 + 4 * s].bitcast(I32) for s in range(SL)]
            hot = [arena[:, 4224 + 128 * k:4352 + 128 * k] for k in range(4)]
            s_hout, s_z0, s_seen = sem("h_out"), sem("sums_zeroed"), sem("indices_seen")
            in_ready = [sem(f"edges_in{s}") for s in range(SL)]
            gathered = [sem(f"gathered{s}") for s in range(SL)]
            added = [sem(f"added{s}") for s in range(SL)]
            message = [sem(f"message{s}") for s in range(SL)]
            slot_free = [sem(f"slot_free{s}") for s in range(SL)]
            hot_ready, product, summed = sem("dst_hot_ready"), sem("block_product"), sem("block_summed")
            block = ctx_block("edges")
            attr_v = edge_attr.rearrange("(g k p) c -> g p k c", k=4, p=P)

            def table(eng, g):
                base = eng.value_load(block_tab[0:1, bass.ds(g * 4, 1)], min_val=0, max_val=NG * NB)
                end = eng.value_load(block_tab[0:1, bass.ds(g * 4 + 1, 1)], min_val=1, max_val=NG * NB)
                return base, end

            @block.sync
            def _(sp):
                sp.dma_start(h_dram.rearrange("(b p) c -> p b c", p=P), y[:, :, :]).then_inc(s_hout, 16)
                with sp.Fori(0, NG // SL) as j:
                    for s in range(SL):
                        sp.wait_ge(slot_free[s], j + 1)
                        sp.dma_start(attr[s].rearrange("p (k c) -> p k c", c=P),
                                     attr_v[bass.ds(j * SL + s, 1)].rearrange("o p k c -> (o p) k c")).then_inc(in_ready[s], 16)
                        sp.dma_start(idx[s], src_groups[bass.ds(j * SL + s, 1)].rearrange("o p k -> (o p) k")).then_inc(in_ready[s], 16)
                sp.wait_ge(s_hout, 16)

            @block.gpsimd
            def _(po):
                po.wait_ge(s_hout, 16)
                with po.Fori(0, NG // SL) as j:
                    for s in range(SL):
                        po.wait_ge(in_ready[s], 32 * (j + 1))
                        po.sem_inc(s_seen, 1)
                        for k in range(4):
                            nc.gpsimd.indirect_dma_start(got[s][:, P * k:P * k + P], None, h_dram,
                                                         bass.IndirectOffsetOnAxis(ap=idx[s][:, k:k + 1], axis=0))\
                                .then_inc(gathered[s], 16)

            @block.scalar
            def _(act):
                with act.Fori(0, NG // SL) as j:
                    for s in range(SL):
                        act.wait_ge(added[s], j + 1)
                        nc.scalar.activation(got[s], got[s], ACT.Relu).then_inc(message[s], 1)

            @block.vector
            def _(dve):
                nc.vector.memset(zT[:, :], 0.0).then_inc(s_z0, 1)
                dve.sem_inc(summed, 1)
                dve.wait_ge(s_z0, 1)
                with dve.Fori(0, NG // SL) as j:
                    for s in range(SL):
                        g = j * SL + s
                        dve.wait_ge(in_ready[s], 32 * (j + 1))
                        dve.wait_ge(gathered[s], 64 * (j + 1))
                        nc.vector.tensor_tensor(got[s], got[s], attr[s], ALU.add).then_inc(added[s], 1)
                        base, end = table(dve, g)
                        shift = dve.value_load(block_tab[0:1, bass.ds(g * 4 + 2, 1)], min_val=-NG * NB, max_val=NB)
                        with dve.Fori(base, end) as step:
                            b = nc.s_assert_within(step + shift, 0, NB - 1, skip_runtime_bounds_check_because="the table holds blocks only")
                            dve.wait_ge(product, step + 1)
                            for k in range(4):
                                last = nc.vector.tensor_scalar(hot[k], iota_f[:, :], dcol[:, bass.ds(g * 4 + k, 1)],
                                                               neg128[:, bass.ds(b, 1)], ALU.subtract,
                                                               ALU.is_equal)
                            last.then_inc(hot_ready, 1)
                            dve.wait_ge(product, step + 2)
                            dve.wait_ge(summed, step + 1)
                            nc.vector.tensor_tensor(zT[:, bass.ds(b * P, P)], ps[:, 0, 0:P],
                                                    zT[:, bass.ds(b * P, P)], ALU.add).then_inc(summed, 1)

            @block.tensor
            def _(pe):
                pe.sem_inc(product, 1)
                for s in range(SL):
                    pe.sem_inc(slot_free[s], 1)
                with pe.Fori(0, NG // SL) as j:
                    for s in range(SL):
                        base, end = table(pe, j * SL + s)
                        with pe.Fori(base, end) as step:
                            pe.wait_ge(message[s], j + 1)
                            pe.wait_ge(hot_ready, step + 1)
                            pe.wait_ge(summed, step + 1)
                            for k in range(4):
                                mm = nc.tensor.matmul(ps[:, 0, 0:P], hot[k], got[s][:, P * k:P * k + P],
                                                      start=(k == 0), stop=(k == 3))
                            mm.then_inc(product, 1)
                        pe.drain().then_inc(slot_free[s], 1)

            block_end(block)

        def norm_constants():
            s_ch, s_sq = sem("bn_chain"), sem("bn_sqrt")
            block = ctx_block("bn_consts")
            names = ["g", "b1", "b2"]

            @block.vector
            def _(dve):
                done = [0]

                def chain(ins):
                    done[0] += 1
                    ins.then_inc(s_ch, 1)
                    dve.wait_ge(s_ch, done[0])

                for k, nm in enumerate(names):
                    chain(nc.vector.tensor_scalar(small[:, 400 + k:401 + k], C[nm + "_v"], BN_EPS, None, ALU.add))
                dve.wait_ge(s_sq, 1)
                chain(nc.vector.reciprocal(small[:, 408:411], small[:, 404:407]))
                for k, nm in enumerate(names):
                    chain(nc.vector.tensor_tensor(bn_scale[k], small[:, 408 + k:409 + k], C[nm + "_g"], ALU.mult))
                    chain(nc.vector.tensor_tensor(small[:, 412:413], bn_scale[k], C[nm + "_m"], ALU.mult))
                    chain(nc.vector.tensor_tensor(bn_shift[k], C[nm + "_b"], small[:, 412:413], ALU.subtract))
                chain(nc.vector.tensor_tensor(small[:, 413:414], bn_scale[1], C["ginb"], ALU.mult))
                chain(nc.vector.tensor_tensor(shift1, small[:, 413:414], bn_shift[1], ALU.add))
                chain(nc.vector.tensor_tensor(small[:, 414:415], bn_scale[2], C["fb2"], ALU.mult))
                chain(nc.vector.tensor_tensor(shift2, small[:, 414:415], bn_shift[2], ALU.add))

            @block.scalar
            def _(act):
                act.wait_ge(s_ch, 3)
                nc.scalar.activation(small[:, 404:407], small[:, 400:403], ACT.Sqrt).then_inc(s_sq, 1)
                act.wait_ge(s_sq, 1)

            block_end(block)

        bn_scale = [small[:, 420 + k:421 + k] for k in range(3)]
        bn_shift = [small[:, 424 + k:425 + k] for k in range(3)]
        shift1, shift2 = small[:, 428:429], small[:, 429:430]

        def add_nodes(name, a, b, target):
            s_d = sem(name)
            block = ctx_block(name)

            @block.vector
            def _(dve):
                nc.vector.tensor_tensor(target, a, b, ALU.add).then_inc(s_d, 1)
                dve.wait_ge(s_d, 1)

            block_end(block)

        open_blocks = []

        def ctx_block(name):
            b = nc.Block(name, no_gpsimd_drain=False)
            open_blocks.append(b)
            return b.__enter__()

        def block_end(_):
            open_blocks.pop().__exit__(None, None, None)
            if len(stage_sems) > 130:
                nc.clear_and_free_semaphores(list(stage_sems))
                nc.all_engine_barrier()
                stage_sems.clear()

        load_and_tables()
        build_adjacency()
        self_loops("loops_on", 1)
        layernorm("ln0")
        for l in range(3):
            gat_layer(l)
            if l < 2:
                turn_y(f"turn{l}", y, yT)
        add_y_to_x("add0")
        self_loops("loops_off", -1)

        layernorm("ln1")
        rdeg = arena[:, 0:ND]
        degrees("deg", rdeg)
        neighbour_sums("sage1", y, zT, (ALU.mult, rdeg))
        dense("sage1_lin", [[([(W["sWs1"], yT), (W["sWn1"], zT)], (ACT.Relu, C["sb1"], 1.0, yT))]])
        node_major("sage1_back", yT[:, :], y, False)
        neighbour_sums("sage2", y, zT, (ALU.mult, rdeg))
        dense("sage2_lin", [[([(W["sWs2"], yT), (W["sWn2"], zT)], (ACT.Identity, C["sb2"], 1.0, yT))]])
        node_major("sage2_back", yT[:, :], x, True)

        layernorm("ln2")
        norm_constants()
        edge_messages()
        add_nodes("gine_h", zN, y[:, :, :], zN)
        turn_y("gine_turn", zN, arena[:, 0:NP])
        hid = [arena[:, 3200:3200 + NP], zT]
        uT = arena[:, 0:NP]
        dense("gine_bn", [
            [([(ident[:, :], uT)], (ACT.Relu, bn_shift[0], bn_scale[0], zT))],
            [([(W["ginW"], zT), (ident[:, :], yT)], (ACT.Identity, shift1, bn_scale[1], yT))],
            [([(W["f1"][:, 0:P], yT)], (ACT.Relu, C["fb1a"], 1.0, arena[:, 0:NP])),
             ([(W["f1"][:, P:2 * P], yT)], (ACT.Relu, C["fb1b"], 1.0, arena[:, NP:2 * NP]))],
            [([(W["f2a"], arena[:, 0:NP]), (W["f2b"], arena[:, NP:2 * NP]), (ident[:, :], yT)],
              (ACT.Identity, shift2, bn_scale[2], zT))]])
        node_major("gine_back", zT[:, :], x, True)

        layernorm("ln3")
        neighbour_sums("gin1", y, zT, (ALU.add, yT))
        hT = [arena[:, 0:NP], arena[:, NP:2 * NP]]
        yF = y[:, :, :].rearrange("p b c -> p (b c)")
        dense("gin1_lin", [
            [([(W["w1a"][:, 0:P], zT)], (ACT.Relu, C["b1a0"], 1.0, yF)),
             ([(W["w1a"][:, P:2 * P], zT)], (ACT.Relu, C["b1a1"], 1.0, yT))],
            [([(W["w2a0"][:, 0:P], yF), (W["w2a1"][:, 0:P], yT)], (ACT.Relu, C["b2a0"], 1.0, hT[0])),
             ([(W["w2a0"][:, P:2 * P], yF), (W["w2a1"][:, P:2 * P], yT)], (ACT.Relu, C["b2a1"], 1.0, hT[1]))]], clear=hT)
        node_major("gin2_back0", hT[0], y, False)
        neighbour_sums("gin2a", y, zT, (ALU.add, hT[0]))
        node_major("gin2_back1", hT[1], y, False)
        neighbour_sums("gin2b", y, yT, (ALU.add, hT[1]))
        dense("gin2_lin", [
            [([(W["w1b0"][:, 0:P], zT), (W["w1b1"][:, 0:P], yT)], (ACT.Relu, C["b1b0"], 1.0, hT[0])),
             ([(W["w1b0"][:, P:2 * P], zT), (W["w1b1"][:, P:2 * P], yT)], (ACT.Relu, C["b1b1"], 1.0, hT[1]))],
            [([(W["w2b0"], hT[0]), (W["w2b1"], hT[1])], (ACT.Identity, C["b2b"], 1.0, zT))]])
        node_major("out_back", zT[:, :], x, True, store=out)


def kernel(**inputs):
    import numpy as _np
    import concourse.bacc as _bacc
    from concourse import mybir as _mybir
    from concourse.bass_utils import run_bass_kernel_spmd as _run

    a = {k: _np.asarray(v) for k, v in inputs.items()}

    def pad(v, n, value):
        full = _np.full((n,) + v.shape[1:], value, v.dtype)
        full[:v.shape[0]] = v
        return full

    dst = pad(a["dst"], EP, PAD_DST)
    src = pad(a["src"], EP, 0)
    weights = {
        "gatW": _np.concatenate(list(a["L0_gnn_Ws"]), 1), "sWs1": a["L1_gnn_W_self1"], "sWn1": a["L1_gnn_W_neigh1"],
        "sWs2": a["L1_gnn_W_self2"], "sWn2": a["L1_gnn_W_neigh2"], "ginW": a["L2_gnn_gin_W"], "f1": a["L2_gnn_ffn_W1"],
        "f2a": a["L2_gnn_ffn_W2"][:P], "f2b": a["L2_gnn_ffn_W2"][P:], "w1a": a["L3_gnn_W1a"],
        "w2a0": a["L3_gnn_W2a"][:P], "w2a1": a["L3_gnn_W2a"][P:], "w1b0": a["L3_gnn_W1b"][:P],
        "w1b1": a["L3_gnn_W1b"][P:], "w2b0": a["L3_gnn_W2b"][:P], "w2b1": a["L3_gnn_W2b"][P:]}
    col = {
        "sb1": a["L1_gnn_b1"], "sb2": a["L1_gnn_b2"], "ginb": a["L2_gnn_gin_b"], "fb1a": a["L2_gnn_ffn_b1"][:P],
        "fb1b": a["L2_gnn_ffn_b1"][P:], "fb2": a["L2_gnn_ffn_b2"], "b1a0": a["L3_gnn_b1a"][:P],
        "b1a1": a["L3_gnn_b1a"][P:], "b2a0": a["L3_gnn_b2a"][:P], "b2a1": a["L3_gnn_b2a"][P:],
        "b1b0": a["L3_gnn_b1b"][:P], "b1b1": a["L3_gnn_b1b"][P:], "b2b": a["L3_gnn_b2b"]}
    for short, long in (("g", "gin_bn"), ("b1", "bn1"), ("b2", "bn2")):
        for k in "gbmv":
            col[f"{short}_{k}"] = a[f"L2_gnn_{long}_{k}"]
    for l in range(3):
        col[f"adst{l}"] = a["L0_gnn_att_dst"][l]
    arrays = {
        "x_in": pad(a["x"], NP, 0).reshape(NB, P, P).transpose(1, 0, 2),
        "dst_units": dst.reshape(UP, UJ * UE),
        "dst_cols": dst.reshape(NC, P).T,
        "src_cols": src.reshape(NC, P).T,
        "src_groups": src.reshape(NG, 4, P).transpose(0, 2, 1),
        "edge_attr": pad(a["edge_attr_128"], EP, 0),
        "weights": _np.concatenate([weights[n] for n, _ in WEIGHTS], 1),
        "columns": _np.stack([col[n] for n in COLUMNS], 1),
        "rows": _np.concatenate([a["L0_gnn_att_src"], a["L0_gnn_att_dst"], a["L0_gnn_bias"]], 0),
    }
    arrays = {k: _np.ascontiguousarray(v) for k, v in arrays.items()}
    nc = _bacc.Bacc("TRN2", target_bir_lowering=False, num_devices=1)
    args = [nc.dram_tensor(k, v.shape, _mybir.dt.from_np(v.dtype), kind="ExternalInput").ap() for k, v in arrays.items()]
    out = nc.dram_tensor("out_0_dram", (P, NB, P), F32, kind="ExternalOutput").ap()
    gnn_stack(nc, *args, out)
    r = _run(nc, [arrays], core_ids=[0])
    got = r.results[0]["out_0_dram"]
    return _np.ascontiguousarray(got.transpose(1, 0, 2).reshape(NP, P)[:N])
```
